# Optimizing a Trainium2 kernel written in Bass

```python
import numpy as np
import jax
import jax.numpy as jnp

def _softmax(x, axis=-1):
    return jax.nn.softmax(x, axis=axis)

def _gelu(x):
    return jax.nn.gelu(x, approximate=True)

def _silu(x):
    return jax.nn.silu(x)

def _sigmoid(x):
    return jax.nn.sigmoid(x)

def _layernorm(x, axis=-1, eps=1e-05):
    m = jnp.mean(x, axis=axis, keepdims=True)
    v = jnp.var(x, axis=axis, keepdims=True)
    return (x - m) / jnp.sqrt(v + eps)

def _scatter_add(tgt, idx, src, axis=0):
    return tgt.at[idx].add(src)

def _segment_sum(src, seg, n):
    return jax.ops.segment_sum(src, seg, n)
kernel_name = 'mk_cond_resid_d2_seqx_r8_b8192c'

def setup_inputs(seed: int=0):
    np.random.seed(seed)
    _w = jnp.asarray

    def _rec_inputs():
        import jax
        import jax.numpy as jnp
        _rk = jax.random.key(seed)
        x = -0.000125 + 0.9999 * jax.random.normal(jax.random.fold_in(_rk, 1), (8, 128, 512), jnp.float32)
        _lenS = 128 - jax.random.randint(jax.random.fold_in(_rk, 7), (8,), 0, max(1, 128 // 4) + 1, jnp.int32)
        _lenS2 = 128 - jax.random.randint(jax.random.fold_in(_rk, 8), (8,), 0, max(1, 128 // 4) + 1, jnp.int32)
        itok_B_0_7 = jax.random.randint(jax.random.fold_in(_rk, 11), (8,), 0, 8, jnp.int32)
        condB_scale = 0.000342416 + 0.0128191 * jax.random.normal(jax.random.fold_in(_rk, 12), (8,), jnp.float32)
        itok_Bx4096x4096_0_255 = jax.random.randint(jax.random.fold_in(_rk, 13), (8, 512, 512), 0, 32, jnp.int32)
        condB_wscale = jax.random.uniform(jax.random.fold_in(_rk, 14), (8,), jnp.float32, 0.0, 0.00091742)
        itok_Bx4096_0_255 = jax.random.randint(jax.random.fold_in(_rk, 16), (8, 512), 0, 32, jnp.int32)
        condB_bscale = jax.random.uniform(jax.random.fold_in(_rk, 17), (8,), jnp.float32, 0.0, 0.000800939)
        return (x, itok_B_0_7, condB_scale, itok_Bx4096x4096_0_255, condB_wscale, itok_Bx4096_0_255, condB_bscale, _lenS)
    x, itok_B_0_7, condB_scale, itok_Bx4096x4096_0_255, condB_wscale, itok_Bx4096_0_255, condB_bscale, _lenS = _rec_inputs()

    def _L0_cond_setup():
        import jax, jax.numpy as jnp
        import numpy as np
        TOP_K = 2
        LANG_BIAS = 5.0
        SCALING = 32.0 / 16.0
        LANGUAGE_PAD_ID = -1
        key = jax.random.key(seed)
        ks = jax.random.split(key, 6)
        B, T, D, O, E, R = (4, 256, 512, 512, 8, 16)
        x = jax.random.normal(ks[0], (B, T, D), dtype=jnp.float32)
        language_ids = jax.random.randint(ks[1], (B,), 0, E).astype(jnp.int64)
        W = jax.random.normal(ks[2], (O, D), dtype=jnp.float32) * (1.0 / np.sqrt(D))
        Wr = jax.random.normal(ks[3], (E, D), dtype=jnp.float32) * (1.0 / np.sqrt(D))
        A = jax.random.normal(ks[4], (E, R, D), dtype=jnp.float32) * (1.0 / np.sqrt(D))
        Bm = jax.random.normal(ks[5], (O, R), dtype=jnp.float32) * 0.0
        Bm = jnp.broadcast_to(Bm, (E, O, R)) + jax.random.normal(ks[5], (E, O, R), dtype=jnp.float32) * 0.02
        return {'x': x, 'language_ids': language_ids, 'W': W, 'Wr': Wr, 'A': A, 'B': Bm}
    _L0_cond_all = _L0_cond_setup()
    _L0_cond_in = {k: v for k, v in _L0_cond_all.items() if k in ('W', 'Wr', 'A', 'B')}
    del _L0_cond_all

    def _L1_cond_setup():
        import jax, jax.numpy as jnp
        import numpy as np
        key = jax.random.key(seed)
        ks = jax.random.split(key, 10)
        N, OUT, IN = (8, 512, 512)
        B, S = (8, 256)
        return {'x': jax.random.normal(ks[0], (B, S, IN), dtype=jnp.float32), 'weight': jax.random.normal(ks[1], (OUT, IN), dtype=jnp.float32) * 0.02, 'bias': jax.random.normal(ks[2], (OUT,), dtype=jnp.float32) * 0.02, 'scale': jax.random.normal(ks[3], (N,), dtype=jnp.float32) * 0.01, 'wq': jax.random.randint(ks[4], (N, OUT, IN), 0, 32, dtype=jnp.int32), 'wscale': jax.random.uniform(ks[5], (N,), dtype=jnp.float32) * 0.001, 'wzp': jax.random.randint(ks[6], (N,), 0, 32, dtype=jnp.int32), 'bq': jax.random.randint(ks[7], (N, OUT), 0, 32, dtype=jnp.int32), 'bscale': jax.random.uniform(ks[8], (N,), dtype=jnp.float32) * 0.001, 'bzp': jax.random.randint(ks[9], (N,), 0, 32, dtype=jnp.int32)}
    _L1_cond_all = _L1_cond_setup()
    _L1_cond_in = {k: v for k, v in _L1_cond_all.items() if k in ('weight', 'bias')}
    del _L1_cond_all
    return {'x': x, 'itok_B_0_7': itok_B_0_7, 'condB_scale': condB_scale, 'itok_Bx4096x4096_0_255': itok_Bx4096x4096_0_255, 'condB_wscale': condB_wscale, 'itok_Bx4096_0_255': itok_Bx4096_0_255, 'condB_bscale': condB_bscale, '_lenS': _lenS, 'L0_cond_W': _L0_cond_in['W'], 'L0_cond_Wr': _L0_cond_in['Wr'], 'L0_cond_A': _L0_cond_in['A'], 'L0_cond_B': _L0_cond_in['B'], 'L1_cond_weight': _L1_cond_in['weight'], 'L1_cond_bias': _L1_cond_in['bias']}

def reference(x, itok_B_0_7, condB_scale, itok_Bx4096x4096_0_255, condB_wscale, itok_Bx4096_0_255, condB_bscale, _lenS, L0_cond_W, L0_cond_Wr, L0_cond_A, L0_cond_B, L1_cond_weight, L1_cond_bias):
    import jax
    import jax.numpy as jnp

    def _L0_cond_ref(x, language_ids, W, Wr, A, B):
        import jax, jax.numpy as jnp
        import numpy as np
        TOP_K = 2
        LANG_BIAS = 5.0
        SCALING = 32.0 / 16.0
        LANGUAGE_PAD_ID = -1
        base = jnp.einsum('btd,od->bto', x, W)
        E = Wr.shape[0]
        logits = jnp.einsum('btd,ed->bte', x.astype(jnp.float32), Wr.astype(jnp.float32))
        expert_targets = language_ids
        valid = expert_targets >= 0
        tgt = jnp.where(valid, expert_targets, 0)
        bias = jax.nn.one_hot(tgt, E, dtype=logits.dtype) * LANG_BIAS
        bias = jnp.where(valid[:, None], bias, 0.0)
        logits = logits + bias[:, None, :]
        topw, topi = jax.lax.top_k(logits, TOP_K)
        weights = jax.nn.softmax(topw, axis=-1)
        gates = jnp.sum(jax.nn.one_hot(topi, E, dtype=weights.dtype) * weights[..., None], axis=-2)
        gates = gates.astype(x.dtype)
        h = jnp.einsum('btd,erd->bter', x, A)
        lora_out = jnp.einsum('bter,bte,eor->bto', h, gates, B)
        return base + SCALING * lora_out

    def _L1_cond_ref(x, weight, bias, scale, wq, wscale, wzp, bq, bscale, bzp):
        import jax, jax.numpy as jnp
        import numpy as np
        f32 = jnp.float32
        dW = jnp.einsum('i,ijk->jk', scale * wscale, wq.astype(f32)) + jnp.dot(scale, wzp.astype(f32))
        W = weight + dW
        db = jnp.einsum('i,ij->j', scale * bscale, bq.astype(f32)) + jnp.dot(scale, bzp.astype(f32))
        b = bias + db
        return jnp.einsum('bsi,oi->bso', x, W) + b
    x = x + _L0_cond_ref(x, itok_B_0_7, L0_cond_W, L0_cond_Wr, L0_cond_A, L0_cond_B)
    x = x + _L1_cond_ref(x, L1_cond_weight, L1_cond_bias, condB_scale, itok_Bx4096x4096_0_255, condB_wscale, _lenS, itok_Bx4096_0_255, condB_bscale, _lenS)
    return x

_drawn_inputs = setup_inputs


def setup_inputs(seed=0):
    import zlib

    import numpy as np

    out = dict(_drawn_inputs(seed))
    spreads = {}
    factors = {'condB_wscale': 200.0, 'condB_bscale': 200.0, 'L0_cond_Wr': 5.127, 'L1_cond_bias': 55.059}
    for name, (base, spread) in spreads.items():
        noise = np.random.default_rng([zlib.crc32(name.encode()), seed]).standard_normal(out[name].shape)
        drawn = base * np.exp(spread * noise) if base else spread * noise
        out[name] = jnp.asarray(drawn.astype(out[name].dtype))
    for name, factor in factors.items():
        out[name] = (out[name] * factor).astype(out[name].dtype)
    return out
```

```python
import concourse.bass as bass
from concourse import mybir
from contextlib import ExitStack


P = 128
BATCH = 8
SEQ = 128
D = 512
E = 8
R = 16
NW = 8
TOP_K = 2
LANG_BIAS = 5.0
SCALING = 2.0
KC = D // P
TOK = BATCH * SEQ
HALVES = 2
TH = TOK // HALVES
TILES = TOK // P
TPH = TILES // HALVES
ER = E * R
AG = ER + E
PAIRS = TILES // 2
WQ_SLOTS = 3
H_BANKS = 3


def cond_resid_kernel(nc, x_t, w0_t, ag_t, b_er, w1_t, wq_t, bias_t, bq_t, floats, ints, out_t):
    fp32 = mybir.dt.float32
    f32r = mybir.dt.float32r
    i32 = mybir.dt.int32
    u32 = mybir.dt.uint32
    ALU = mybir.AluOpType
    ACT = mybir.ActivationFunctionType
    AX = mybir.AxisListType

    ctx = ExitStack()
    with ctx:
        def sb(name, shape, dt=fp32):
            return ctx.enter_context(nc.sbuf_tensor(name, shape, dt))

        def sem(name):
            return ctx.enter_context(nc.semaphore(name))

        res = sb("res", [P, HALVES, KC, TH])
        act_hi = sb("act_hi", [P, 3, KC, TH], f32r)
        act_lo = sb("act_lo", [P, 3, KC, TH], f32r)
        Y_SLOT = [2, 0]
        w0 = sb("w0", [P, KC, D])
        w0_hi = sb("w0_hi", [P, KC, D], f32r)
        w0_lo = sb("w0_lo", [P, KC, D], f32r)
        ag = sb("ag", [P, KC, AG])
        ag_hi = sb("ag_hi", [P, KC, AG], f32r)
        ag_lo = sb("ag_lo", [P, KC, AG], f32r)
        be = sb("be", [P, D])
        be_hi = sb("be_hi", [P, D], f32r)
        be_lo = sb("be_lo", [P, D], f32r)
        w1 = sb("w1", [P, KC, D])
        w1_hi = sb("w1_hi", [P, KC, D], f32r)
        w1_lo = sb("w1_lo", [P, KC, D], f32r)
        wq = sb("wq", [P, WQ_SLOTS, NW, D], i32)
        hx = sb("hx", [P, TILES, AG])
        hg = sb("hg", [P, TILES, ER])
        hgT_hi = sb("hgT_hi", [P, HALVES, TH], f32r)
        hgT_lo = sb("hgT_lo", [P, HALVES, TH], f32r)
        fl = sb("fl", [P, 3, NW])
        it = sb("it", [P, 2, NW], i32)
        bias_o = sb("bias_o", [P, KC])
        bq = sb("bq", [P, KC, NW], i32)
        wcoef = sb("wcoef", [P, NW])
        bcoef = sb("bcoef", [P, NW])
        slen = sb("slen", [P, NW])
        shift = sb("shift", [P, 1])
        bprod = sb("bprod", [P, KC, NW])
        bsum = sb("bsum", [P, KC])
        b1 = sb("b1", [P, KC])
        lane = sb("lane", [P, TOP_K, E])
        lbias = sb("lbias", [P, TILES, E])
        lg = sb("lg", [P, TILES, E])
        top = sb("top", [P, TILES, 8])
        topi = sb("topi", [P, TILES, 8], u32)
        gap = sb("gap", [P, TILES])
        eg = sb("eg", [P, TILES])
        den = sb("den", [P, TILES])
        rden = sb("rden", [P, TILES])
        wts = sb("wts", [P, TILES, TOP_K])
        hot = sb("hot", [P, TILES, TOP_K, E])
        gates = sb("gates", [P, TILES, E])
        ident = sb("ident", [P, P])

        bank = [ctx.enter_context(nc.psum_tensor(f"bank{i}", [P, TH], fp32)) for i in range(8)]
        L0_BANK = [[0, 1, 2, 3], [5, 6, 0, 1]]
        H_BANK = [4 + p % H_BANKS for p in range(PAIRS)]
        T_BANK = 7
        L1_BANK = [[2, 3, 4, 7], [5, 6, 0, 1]]

        x_in = [[sem(f"x_in{h}{k}") for k in range(KC)] for h in range(HALVES)]
        w0_in = [sem(f"w0_in{k}") for k in range(KC)]
        ag_in = sem("ag_in")
        be_in = sem("be_in")
        w1_in = sem("w1_in")
        wq_in = [[sem(f"wq_in{k}{j}") for j in range(2)] for k in range(KC)]
        fl_in = sem("fl_in")
        it_in = sem("it_in")
        bias_in = sem("bias_in")
        bq_in = sem("bq_in")
        out_stored = sem("out_stored")
        x_hi = sem("x_hi")
        w0_hi_s = sem("w0_hi_s")
        ag_hi_s = sem("ag_hi_s")
        be_hi_s = sem("be_hi_s")
        w1_shifted = sem("w1_shifted")
        w1_hi_s = sem("w1_hi_s")
        hx_out = sem("hx_out")
        eg_s = sem("eg_s")
        hgT_hi_s = sem("hgT_hi_s")
        y_hi = sem("y_hi")
        w0_lo_s = sem("w0_lo_s")
        ag_lo_s = sem("ag_lo_s")
        be_lo_s = sem("be_lo_s")
        shift_s = sem("shift_s")
        gap_s = sem("gap_s")
        hg_s = sem("hg_s")
        hgT_lo_s = sem("hgT_lo_s")
        y_s = sem("y_s")
        dw_s = sem("dw_s")
        w1_lo_s = sem("w1_lo_s")
        out_s = sem("out_s")
        dve_step = sem("dve_step")
        x_lo = sem("x_lo")
        y_lo = sem("y_lo")
        lane_s = sem("lane_s")
        ident0 = sem("ident0")
        ident_s = sem("ident_s")
        pair_mm = sem("pair_mm")
        l0_mm = sem("l0_mm")
        hgT_mm = sem("hgT_mm")
        l1_mm = sem("l1_mm")

        block = ctx.enter_context(nc.Block())

        @block.sync
        def _(sp):
            for k in range(KC):
                sp.dma_start(res[:, 0, k, :], x_t[:, 0, k, :]).then_inc(x_in[0][k], 16)
                sp.dma_start(w0[:, k, :], w0_t[:, k, :]).then_inc(w0_in[k], 16)
            sp.dma_start(ag[:, :, :], ag_t).then_inc(ag_in, 16)
            for k in range(KC):
                sp.dma_start(res[:, 1, k, :], x_t[:, 1, k, :]).then_inc(x_in[1][k], 16)
            sp.dma_start(be[:, :], b_er).then_inc(be_in, 16)
            sp.dma_start(w1[:, :, :], w1_t).then_inc(w1_in, 16)
            for k in range(KC):
                if k >= WQ_SLOTS:
                    sp.wait_ge(dw_s, k - WQ_SLOTS + 1)
                for j in range(2):
                    sp.dma_start(wq[:, k % WQ_SLOTS, 4 * j:4 * j + 4, :],
                                 wq_t[:, k, 4 * j:4 * j + 4, :]).then_inc(wq_in[k][j], 16)
            for n in range(HALVES * KC):
                sp.wait_ge(out_s, n + 1)
                sp.dma_start(out_t[:, n // KC, n % KC, :], res[:, n // KC, n % KC, :]).then_inc(out_stored, 16)
            sp.wait_ge(out_stored, 16 * HALVES * KC)

        @block.gpsimd
        def _(pool):
            nc.gpsimd.memset(ident[:, :], 0.0).then_inc(ident0, 1)
            nc.gpsimd.iota(lane[:, :, :], pattern=[[0, TOP_K], [1, E]], base=0, channel_multiplier=0,
                           allow_small_or_imprecise_dtypes=True).then_inc(lane_s, 1)
            pool.wait_ge(ident0, 1)
            nc.gpsimd.affine_select(out=ident[:, :], in_=ident[:, :], compare_op=ALU.not_equal, fill=1.0,
                                    base=0, pattern=[[-1, P]], channel_multiplier=1).then_inc(ident_s, 1)
            for n in range(HALVES * KC):
                h, k = n // KC, n % KC
                pool.wait_ge(x_hi, n + 1)
                nc.gpsimd.tensor_tensor(act_lo[:, h, k, :], res[:, h, k, :], act_hi[:, h, k, :].bitcast(fp32),
                                        ALU.subtract).then_inc(x_lo, 1)
            for n in range(HALVES * KC):
                h, m = n // KC, n % KC
                pool.wait_ge(y_hi, n + 1)
                nc.gpsimd.tensor_tensor(act_lo[:, Y_SLOT[h], m, :], res[:, h, m, :],
                                        act_hi[:, Y_SLOT[h], m, :].bitcast(fp32),
                                        ALU.subtract).then_inc(y_lo, 1)

        @block.scalar
        def _(act):
            act.dma_start(fl[:, :, :], floats.partition_broadcast(P)).then_inc(fl_in, 16)
            act.dma_start(it[:, :, :], ints.partition_broadcast(P)).then_inc(it_in, 16)
            act.dma_start(bias_o[:, :], bias_t).then_inc(bias_in, 16)
            act.dma_start(bq[:, :, :], bq_t).then_inc(bq_in, 16)
            for k in range(KC):
                act.wait_ge(x_in[0][k], 16)
                nc.scalar.copy(act_hi[:, 0, k, :], res[:, 0, k, :]).then_inc(x_hi, 1)
                act.wait_ge(w0_in[k], 16)
                nc.scalar.copy(w0_hi[:, k, :], w0[:, k, :]).then_inc(w0_hi_s, 1)
            act.wait_ge(ag_in, 16)
            nc.scalar.copy(ag_hi[:, :, :], ag[:, :, :]).then_inc(ag_hi_s, 1)
            for k in range(KC):
                act.wait_ge(x_in[1][k], 16)
                nc.scalar.copy(act_hi[:, 1, k, :], res[:, 1, k, :]).then_inc(x_hi, 1)
            act.wait_ge(be_in, 16)
            nc.scalar.copy(be_hi[:, :], be[:, :]).then_inc(be_hi_s, 1)

            def evacuate_pair(p):
                act.wait_ge(pair_mm, p + 1)
                nc.scalar.copy(hx[:, 2 * p:2 * p + 2, :],
                               bank[H_BANK[p]][:, 0:2 * AG].rearrange("p (t c) -> p t c", t=2)).then_inc(hx_out, 1)

            def exp_gap(h):
                act.wait_ge(gap_s, h + 1)
                nc.scalar.activation(eg[:, h * TPH:(h + 1) * TPH], gap[:, h * TPH:(h + 1) * TPH],
                                     ACT.Exp).then_inc(eg_s, 1)

            def split_hgT(h):
                act.wait_ge(hgT_mm, h + 1)
                nc.scalar.copy(hgT_hi[:, h, :], bank[T_BANK][:, :]).then_inc(hgT_hi_s, 1)

            def split_y(n):
                h, m = n // KC, n % KC
                act.wait_ge(y_s, n + 1)
                nc.scalar.copy(act_hi[:, Y_SLOT[h], m, :], res[:, h, m, :]).then_inc(y_hi, 1)

            def split_w1(k):
                act.wait_ge(dw_s, k + 1)
                nc.scalar.copy(w1_hi[:, k, :], w1[:, k, :]).then_inc(w1_hi_s, 1)

            evacuate_pair(0)
            evacuate_pair(1)
            act.wait_ge(w1_in, 16)
            act.wait_ge(shift_s, 1)
            nc.scalar.activation(w1[:, :, :], w1[:, :, :], ACT.Identity, bias=shift[:, 0:1]).then_inc(w1_shifted, 1)
            evacuate_pair(2)
            exp_gap(0)
            evacuate_pair(3)
            exp_gap(1)
            split_hgT(0)
            for n in range(KC):
                split_y(n)
            split_hgT(1)
            split_w1(0)
            split_y(4)
            split_y(5)
            split_w1(1)
            split_y(6)
            split_y(7)
            split_w1(2)
            split_w1(3)

        @block.vector
        def _(dve):
            steps = [0]

            def link(ins):
                steps[0] += 1
                ins.then_inc(dve_step, 1)
                dve.wait_ge(dve_step, steps[0])

            for k in range(KC):
                dve.wait_ge(w0_hi_s, k + 1)
                nc.vector.tensor_tensor(w0_lo[:, k, :], w0[:, k, :], w0_hi[:, k, :].bitcast(fp32),
                                        ALU.subtract).then_inc(w0_lo_s, 1)
            dve.wait_ge(ag_hi_s, 1)
            nc.vector.tensor_tensor(ag_lo[:, :, :], ag[:, :, :], ag_hi[:, :, :].bitcast(fp32),
                                    ALU.subtract).then_inc(ag_lo_s, 1)
            dve.wait_ge(fl_in, 16)
            dve.wait_ge(it_in, 16)
            nc.vector.tensor_tensor(wcoef[:, :], fl[:, 0, :], fl[:, 1, :], ALU.mult)
            nc.vector.tensor_tensor(bcoef[:, :], fl[:, 0, :], fl[:, 2, :], ALU.mult)
            link(nc.vector.tensor_tensor(slen[:, :], fl[:, 0, :], it[:, 1, :], ALU.mult))
            link(nc.vector.reduce_sum(shift[:, 0:1], slen[:, :], axis=AX.X))
            dve.wait_ge(bq_in, 16)
            dve.wait_ge(bias_in, 16)
            nc.vector.tensor_scalar(b1[:, :], bias_o[:, :], shift[:, 0:1], None, ALU.add).then_inc(shift_s, 1)
            link(nc.vector.tensor_tensor(bprod[:, :, :], bq[:, :, :],
                                         bcoef[:, :].unsqueeze(1).to_broadcast([P, KC, NW]), ALU.mult))
            link(nc.vector.reduce_sum(bsum[:, :], bprod[:, :, :], axis=AX.X))
            link(nc.vector.tensor_tensor(b1[:, :], b1[:, :], bsum[:, :], ALU.add))
            dve.wait_ge(lane_s, 1)
            link(nc.vector.tensor_tensor(lbias[:, :, :], lane[:, 0, :].unsqueeze(1).to_broadcast([P, TILES, E]),
                                         it[:, 0, :].unsqueeze(2).to_broadcast([P, TILES, E]), ALU.is_equal))
            link(nc.vector.tensor_scalar(lbias[:, :, :], lbias[:, :, :], LANG_BIAS, None, ALU.mult))
            dve.wait_ge(be_hi_s, 1)
            nc.vector.tensor_tensor(be_lo[:, :], be[:, :], be_hi[:, :].bitcast(fp32), ALU.subtract).then_inc(be_lo_s, 1)

            def route(h):
                ts = slice(h * TPH, (h + 1) * TPH)
                dve.wait_ge(hx_out, 2 * (h + 1))
                link(nc.vector.tensor_tensor(lg[:, ts, :], hx[:, ts, ER:AG], lbias[:, ts, :], ALU.add))
                for n in range(h * TPH, (h + 1) * TPH):
                    last = nc.vector.max(top[:, n, :], lg[:, n, :])
                link(last)
                nc.vector.tensor_tensor(gap[:, ts], top[:, ts, 1], top[:, ts, 0], ALU.subtract).then_inc(gap_s, 1)
                for n in range(h * TPH, (h + 1) * TPH):
                    last = nc.vector.max_index(topi[:, n, :], top[:, n, :], lg[:, n, :])
                link(last)
                nc.vector.tensor_tensor(
                    hot[:, ts, :, :], lane[:, :, :].unsqueeze(1).to_broadcast([P, TPH, TOP_K, E]),
                    topi[:, ts, 0:TOP_K].unsqueeze(3).to_broadcast([P, TPH, TOP_K, E]), ALU.is_equal)
                dve.wait_ge(eg_s, h + 1)
                link(nc.vector.tensor_scalar(den[:, ts], eg[:, ts], 1.0, None, ALU.add))
                link(nc.vector.reciprocal(rden[:, ts], den[:, ts]))
                nc.vector.tensor_scalar(wts[:, ts, 0], rden[:, ts], SCALING, None, ALU.mult)
                link(nc.vector.scalar_tensor_tensor(wts[:, ts, 1], eg[:, ts], SCALING, rden[:, ts],
                                                    ALU.mult, ALU.mult))
                link(nc.vector.tensor_tensor(hot[:, ts, :, :], hot[:, ts, :, :],
                                             wts[:, ts, :].unsqueeze(3).to_broadcast([P, TPH, TOP_K, E]), ALU.mult))
                link(nc.vector.tensor_tensor(gates[:, ts, :], hot[:, ts, 0, :], hot[:, ts, 1, :], ALU.add))
                nc.vector.tensor_tensor(
                    hg[:, ts, :].rearrange("p t (e r) -> p t e r", e=E),
                    hx[:, ts, 0:ER].rearrange("p t (e r) -> p t e r", e=E),
                    gates[:, ts, :].unsqueeze(3).to_broadcast([P, TPH, E, R]), ALU.mult).then_inc(hg_s, 1)

            def hgT_low(h):
                dve.wait_ge(hgT_hi_s, h + 1)
                nc.vector.tensor_tensor(hgT_lo[:, h, :], bank[T_BANK][:, :], hgT_hi[:, h, :].bitcast(fp32),
                                        ALU.subtract).then_inc(hgT_lo_s, 1)

            def add_residual(n):
                h, m = n // KC, n % KC
                dve.wait_ge(l0_mm, n + 1)
                nc.vector.tensor_tensor(res[:, h, m, :], bank[L0_BANK[h][m]][:, :], res[:, h, m, :],
                                        ALU.add).then_inc(y_s, 1)

            def add_deltas(k, i0, i1):
                for i in range(i0, i1):
                    if i % 4 == 0:
                        dve.wait_ge(wq_in[k][i // 4], 16)
                    ins = nc.vector.scalar_tensor_tensor(w1[:, k, :], wq[:, k % WQ_SLOTS, i, :], wcoef[:, i:i + 1],
                                                         w1[:, k, :], ALU.mult, ALU.add)
                    if i < NW - 1:
                        link(ins)
                    else:
                        ins.then_inc(dw_s, 1)

            def w1_low(k):
                dve.wait_ge(w1_hi_s, k + 1)
                nc.vector.tensor_tensor(w1_lo[:, k, :], w1[:, k, :], w1_hi[:, k, :].bitcast(fp32),
                                        ALU.subtract).then_inc(w1_lo_s, 1)

            route(0)
            route(1)
            dve.wait_ge(w1_shifted, 1)
            hgT_low(0)
            add_deltas(0, 0, 4)
            for n in range(KC):
                add_residual(n)
            hgT_low(1)
            add_deltas(0, 4, 8)
            add_residual(4)
            w1_low(0)
            add_deltas(1, 0, 4)
            add_residual(5)
            add_deltas(1, 4, 8)
            add_residual(6)
            w1_low(1)
            add_deltas(2, 0, 4)
            add_residual(7)
            add_deltas(2, 4, 8)
            w1_low(2)
            add_deltas(3, 0, 8)
            w1_low(3)
            for n in range(HALVES * KC):
                h, o = n // KC, n % KC
                dve.wait_ge(l1_mm, n + 1)
                nc.vector.scalar_tensor_tensor(res[:, h, o, :], bank[L1_BANK[h][o]][:, :], b1[:, o:o + 1],
                                               res[:, h, o, :], ALU.add, ALU.add).then_inc(out_s, 1)

        @block.tensor
        def _(pe):
            def mm3(dst, w_hi, w_lo, a_hi, a_lo, first, last):
                nc.tensor.matmul(dst, w_hi, a_hi, start=first, stop=False)
                nc.tensor.matmul(dst, w_hi, a_lo, start=False, stop=False)
                return nc.tensor.matmul(dst, w_lo, a_hi, start=False, stop=last)

            def l0_step(h, m, k):
                mm3(bank[L0_BANK[h][m]][:, :], w0_hi[:, k, m * P:(m + 1) * P], w0_lo[:, k, m * P:(m + 1) * P],
                    act_hi[:, h, k, :], act_lo[:, h, k, :], k == 0, False)

            def lora_step(h, m):
                mm3(bank[L0_BANK[h][m]][:, :], be_hi[:, m * P:(m + 1) * P], be_lo[:, m * P:(m + 1) * P],
                    hgT_hi[:, h, :], hgT_lo[:, h, :], False, True).then_inc(l0_mm, 1)

            def experts(p):
                if p >= H_BANKS:
                    pe.wait_ge(hx_out, p - H_BANKS + 1)
                for j in range(2):
                    n = 2 * p + j
                    h, c = n // TPH, (n % TPH) * P
                    dst = bank[H_BANK[p]][:, j * AG:(j + 1) * AG]
                    for k in range(KC):
                        last = mm3(dst, act_hi[:, h, k, c:c + P], act_lo[:, h, k, c:c + P],
                                   ag_hi[:, k, :], ag_lo[:, k, :], k == 0, k == KC - 1)
                last.then_inc(pair_mm, 1)

            def transpose_hg(h):
                pe.wait_ge(hg_s, h + 1)
                for j in range(TPH):
                    last = nc.tensor.transpose(bank[T_BANK][:, j * P:(j + 1) * P], hg[:, h * TPH + j, :], ident[:, :])
                last.then_inc(hgT_mm, 1)

            def l1_step(h, o, k):
                s = Y_SLOT[h]
                return mm3(bank[L1_BANK[h][o]][:, :], w1_hi[:, k, o * P:(o + 1) * P], w1_lo[:, k, o * P:(o + 1) * P],
                           act_hi[:, s, k, :], act_lo[:, s, k, :], k == 0, k == KC - 1)

            for k in range(KC):
                pe.wait_ge(w0_hi_s, k + 1)
                pe.wait_ge(x_hi, k + 1)
                pe.wait_ge(w0_lo_s, k + 1)
                pe.wait_ge(x_lo, k + 1)
                for m in range(KC):
                    l0_step(0, m, k)
            pe.wait_ge(ag_hi_s, 1)
            pe.wait_ge(ag_lo_s, 1)
            experts(0)
            experts(1)
            pe.wait_ge(x_hi, 2 * KC)
            pe.wait_ge(x_lo, 2 * KC)
            experts(2)
            experts(3)
            pe.wait_ge(hx_out, 2)
            for k in range(KC):
                l0_step(1, 0, k)
            pe.wait_ge(ident_s, 1)
            transpose_hg(0)
            pe.wait_ge(be_hi_s, 1)
            pe.wait_ge(be_lo_s, 1)
            pe.wait_ge(hgT_lo_s, 1)
            for m in range(KC):
                lora_step(0, m)
            transpose_hg(1)
            pe.wait_ge(hx_out, 3)
            for k in range(KC):
                l0_step(1, 1, k)
            pe.wait_ge(hgT_lo_s, 2)
            lora_step(1, 0)
            lora_step(1, 1)
            for m in range(2, KC):
                pe.wait_ge(y_s, m - 1)
                for k in range(KC):
                    l0_step(1, m, k)
                lora_step(1, m)
            pe.wait_ge(y_s, KC)
            pe.wait_ge(hx_out, PAIRS)
            pe.wait_ge(y_lo, KC)
            for k in range(KC):
                pe.wait_ge(w1_hi_s, k + 1)
                pe.wait_ge(w1_lo_s, k + 1)
                for o in range(KC):
                    last = l1_step(0, o, k)
                    if k == KC - 1:
                        last.then_inc(l1_mm, 1)
            pe.wait_ge(y_lo, 2 * KC)
            for o in range(KC):
                for k in range(KC):
                    last = l1_step(1, o, k)
                last.then_inc(l1_mm, 1)


def kernel(x, itok_B_0_7, condB_scale, itok_Bx4096x4096_0_255, condB_wscale, itok_Bx4096_0_255, condB_bscale,
           _lenS, L0_cond_W, L0_cond_Wr, L0_cond_A, L0_cond_B, L1_cond_weight, L1_cond_bias):
    import numpy as np
    import concourse.bacc as bacc
    from concourse import mybir as mb
    from concourse.bass_utils import run_bass_kernel_spmd

    def rows_on_partitions(m):
        return np.asarray(m).reshape(KC, P, -1).transpose(1, 0, 2)

    x = np.asarray(x)
    ag = np.concatenate([np.asarray(L0_cond_A).reshape(ER, D), np.asarray(L0_cond_Wr)], axis=0)
    wq = np.asarray(itok_Bx4096x4096_0_255)
    arrays = {
        "x_t": x.reshape(HALVES, TH, KC, P).transpose(3, 0, 2, 1),
        "w0_t": rows_on_partitions(np.asarray(L0_cond_W).T),
        "ag_t": rows_on_partitions(ag.T),
        "b_er": np.asarray(L0_cond_B).transpose(0, 2, 1).reshape(ER, D),
        "w1_t": rows_on_partitions(np.asarray(L1_cond_weight).T),
        "wq_t": wq.transpose(2, 0, 1).reshape(KC, P, NW, D).transpose(1, 0, 2, 3),
        "bias_t": np.asarray(L1_cond_bias).reshape(KC, P).T,
        "bq_t": np.asarray(itok_Bx4096_0_255).reshape(NW, KC, P).transpose(2, 1, 0),
        "floats": np.stack([np.asarray(condB_scale), np.asarray(condB_wscale), np.asarray(condB_bscale)]),
        "ints": np.stack([np.asarray(itok_B_0_7), np.asarray(_lenS)]),
    }
    nc = bacc.Bacc("TRN2", target_bir_lowering=False, num_devices=1)
    args = []
    for name in arrays:
        arrays[name] = np.ascontiguousarray(arrays[name])
        a = arrays[name]
        args.append(nc.dram_tensor(name, a.shape, mb.dt.from_np(a.dtype), kind="ExternalInput").ap())
    out = nc.dram_tensor("out_t", (P, HALVES, KC, TH), mb.dt.float32, kind="ExternalOutput").ap()
    cond_resid_kernel(nc, *args, out)
    r = run_bass_kernel_spmd(nc, [arrays], core_ids=[0])
    out_t = r.results[0]["out_t"]
    return out_t.transpose(1, 3, 2, 0).reshape(BATCH, SEQ, D)
```

```python
import concourse.bass as bass
from concourse import mybir
from contextlib import ExitStack


P = 128
BATCH = 8
SEQ = 128
D = 512
E = 8
R = 16
NW = 8
TOP_K = 2
LANG_BIAS = 5.0
SCALING = 2.0
KC = D // P
TOK = BATCH * SEQ
HALVES = 2
TH = TOK // HALVES
TILES = TOK // P
TPH = TILES // HALVES
ER = E * R
AG = ER + E
PAIRS = KC // 2
PD = 2 * D
QUADS = NW // 2
WQ_PIECES = PAIRS * QUADS
WQ_SLOTS = 6
H_BANKS = 3
WARM = 9


def cond_resid_kernel(nc, x_t, w0_t, ag_t, b_er, w1_t, wq_t, small_f, small_i, out_t):
    fp32 = mybir.dt.float32
    f32r = mybir.dt.float32r
    bf16 = mybir.dt.bfloat16
    i32 = mybir.dt.int32
    u32 = mybir.dt.uint32
    ALU = mybir.AluOpType
    ACT = mybir.ActivationFunctionType
    AX = mybir.AxisListType

    ctx = ExitStack()
    with ctx:
        def sb(name, shape, dt=fp32):
            return ctx.enter_context(nc.sbuf_tensor(name, shape, dt))

        def sem(name):
            return ctx.enter_context(nc.semaphore(name))

        res = sb("res", [P, HALVES, KC, TH])
        act_hi = sb("act_hi", [P, 3, KC, TH], f32r)
        act_lo = sb("act_lo", [P, 3, KC, TH], f32r)
        Y_SLOT = [2, 0]
        w0 = sb("w0", [P, KC, D])
        w0_hi = sb("w0_hi", [P, KC, D], f32r)
        w0_lo = sb("w0_lo", [P, KC, D], f32r)
        ag = sb("ag", [P, KC, AG])
        ag_hl = sb("ag_hl", [P, KC, 2, AG], f32r)
        be = sb("be", [P, D])
        be_hi = sb("be_hi", [P, D], f32r)
        be_lo = sb("be_lo", [P, D], f32r)
        w1 = sb("w1", [P, PAIRS, PD])
        w1_hi = sb("w1_hi", [P, PAIRS, PD], f32r)
        w1_lo = sb("w1_lo", [P, PAIRS, PD], f32r)
        wq = sb("wq", [P, WQ_SLOTS, 2, PD], i32)
        wqf = wq[:, :, :, :].bitcast(fp32)
        hx = sb("hx", [P, TILES, 2, AG])
        hg = sb("hg", [P, TILES, ER])
        hgT_hi = sb("hgT_hi", [P, HALVES, TH], f32r)
        hgT_lo = sb("hgT_lo", [P, HALVES, TH], f32r)
        sf = sb("sf", [P, 3 * NW + KC])
        scale, wscale, bscale = (sf[:, i * NW:(i + 1) * NW] for i in range(3))
        bias_o = sf[:, 3 * NW:3 * NW + KC]
        si = sb("si", [P, 2 * NW + KC * NW], i32)
        expert = si[:, 0:NW]
        length = si[:, NW:2 * NW]
        bq = si[:, 2 * NW:2 * NW + KC * NW].rearrange("p (k i) -> p k i", k=KC)
        wcoef = sb("wcoef", [P, NW])
        bcoef = sb("bcoef", [P, NW])
        slen = sb("slen", [P, NW])
        shift = sb("shift", [P, 1])
        bprod = sb("bprod", [P, KC, NW])
        bsum = sb("bsum", [P, KC])
        b1 = sb("b1", [P, KC])
        lane = sb("lane", [P, TOP_K, E])
        lbias = sb("lbias", [P, TILES, E])
        lg0 = sb("lg0", [P, TILES, E])
        lg = sb("lg", [P, TILES, E])
        top = sb("top", [P, TILES, 8])
        topi = sb("topi", [P, TILES, 8], u32)
        gap = sb("gap", [P, TILES])
        eg = sb("eg", [P, TILES])
        den = sb("den", [P, TILES])
        rden = sb("rden", [P, TILES])
        wts = sb("wts", [P, TILES, TOP_K])
        hot = sb("hot", [P, TILES, TOP_K, E])
        gates = sb("gates", [P, TILES, E])
        ident = sb("ident", [P, P])
        zeros = sb("zeros", [P, TH], bf16)
        tab = sb("tab", [P, 1])

        bank = [ctx.enter_context(nc.psum_tensor(f"bank{i}", [P, TH], fp32)) for i in range(8)]
        L0_BANK = [[0, 1, 2, 3], [6, 4, 5, 0]]
        H_BANK = [4 + n % H_BANKS for n in range(TILES)]
        T_BANK = 7
        L1_BANK = [[1, 2, 3, 7], [6, 4, 5, 0]]

        x_in = [[sem(f"x_in{h}{k}") for k in range(KC)] for h in range(HALVES)]
        w0_in = [sem(f"w0_in{k}") for k in range(KC)]
        ag_in = sem("ag_in")
        be_in = sem("be_in")
        w1_in = [sem(f"w1_in{q}") for q in range(PAIRS)]
        wq_in = [sem(f"wq_in{j}") for j in range(WQ_PIECES)]
        sf_in = sem("sf_in")
        si_in = sem("si_in")
        out_stored = sem("out_stored")
        x_hi = sem("x_hi")
        ag_hi_s = sem("ag_hi_s")
        be_hi_s = sem("be_hi_s")
        w1_shifted = sem("w1_shifted")
        w1_hi_s = sem("w1_hi_s")
        hx_out = sem("hx_out")
        wq_scaled = sem("wq_scaled")
        eg_s = sem("eg_s")
        hgT_hi_s = sem("hgT_hi_s")
        y_hi = sem("y_hi")
        zeros_s = sem("zeros_s")
        w0_hi_s = sem("w0_hi_s")
        w0_lo_s = sem("w0_lo_s")
        x1_lo = sem("x1_lo")
        ag_lo_s = sem("ag_lo_s")
        be_lo_s = sem("be_lo_s")
        shift_s = sem("shift_s")
        gap_s = sem("gap_s")
        hg_s = sem("hg_s")
        hgT_lo_s = sem("hgT_lo_s")
        y_s = sem("y_s")
        dw_i = sem("dw_i")
        w1_lo_s = sem("w1_lo_s")
        out_s = sem("out_s")
        dve_step = sem("dve_step")
        x0_lo = sem("x0_lo")
        y_lo = sem("y_lo")
        lane_s = sem("lane_s")
        ident0 = sem("ident0")
        ident_s = sem("ident_s")
        hsum_s = sem("hsum_s")
        pool_sum = sem("pool_sum")
        tile_mm = sem("tile_mm")
        l0_mm = sem("l0_mm")
        hgT_mm = sem("hgT_mm")
        l1_mm = sem("l1_mm")

        POOL_DELTAS = [2, 3, 4, 5]

        def delta(q, i):
            return (q * QUADS + i // 2) % WQ_SLOTS, i % 2

        ADDS = [2, 5, 5, 4] + [5 + 2 * (j + 1) for j in range(QUADS)]
        DW_DONE = [5, 5 + NW]

        block = ctx.enter_context(nc.Block())

        @block.sync
        def _(sp):
            def load_wq(j):
                if j >= WQ_SLOTS:
                    sp.wait_ge(dw_i, ADDS[j - WQ_SLOTS])
                q, d = j // QUADS, 2 * (j % QUADS)
                sp.dma_start(wq[:, j % WQ_SLOTS, :, :], wq_t[:, q, d:d + 2, :]).then_inc(wq_in[j], 16)

            for k in range(KC):
                sp.dma_start(res[:, 0, k, :], x_t[:, 0, k, :]).then_inc(x_in[0][k], 16)
                sp.dma_start(w0[:, k, :], w0_t[:, k, :]).then_inc(w0_in[k], 16)
            sp.dma_start(ag[:, :, :], ag_t).then_inc(ag_in, 16)
            sp.dma_start(sf[:, :], small_f).then_inc(sf_in, 16)
            sp.dma_start(si[:, :], small_i).then_inc(si_in, 16)
            sp.dma_start(w1[:, 0, :], w1_t[:, 0, :]).then_inc(w1_in[0], 16)
            load_wq(0)
            for k in range(KC):
                sp.dma_start(res[:, 1, k, :], x_t[:, 1, k, :]).then_inc(x_in[1][k], 16)
            load_wq(1)
            sp.dma_start(be[:, :], b_er).then_inc(be_in, 16)
            load_wq(2)
            load_wq(3)
            sp.dma_start(w1[:, 1, :], w1_t[:, 1, :]).then_inc(w1_in[1], 16)
            for j in range(QUADS, WQ_PIECES):
                load_wq(j)
            for n in range(HALVES * KC):
                sp.wait_ge(out_s, n + 1)
                sp.dma_start(out_t[:, n // KC, n % KC, :], res[:, n // KC, n % KC, :]).then_inc(out_stored, 16)
            sp.wait_ge(out_stored, 16 * HALVES * KC)

        @block.gpsimd
        def _(pool):
            nc.gpsimd.memset(ident[:, :], 0.0).then_inc(ident0, 1)
            nc.gpsimd.iota(lane[:, :, :], pattern=[[0, TOP_K], [1, E]], base=0, channel_multiplier=0,
                           allow_small_or_imprecise_dtypes=True).then_inc(lane_s, 1)
            pool.wait_ge(ident0, 1)
            nc.gpsimd.affine_select(out=ident[:, :], in_=ident[:, :], compare_op=ALU.not_equal, fill=1.0,
                                    base=0, pattern=[[-1, P]], channel_multiplier=1).then_inc(ident_s, 1)
            for k in range(KC):
                pool.wait_ge(x_hi, k + 1)
                nc.gpsimd.tensor_tensor(act_lo[:, 0, k, :], res[:, 0, k, :], act_hi[:, 0, k, :].bitcast(fp32),
                                        ALU.subtract).then_inc(x0_lo, 1)

            def sum_halves(h):
                ts = slice(h * TPH, (h + 1) * TPH)
                pool.wait_ge(hx_out, TPH * (h + 1))
                nc.gpsimd.tensor_tensor(hg[:, ts, :], hx[:, ts, 0, 0:ER], hx[:, ts, 1, 0:ER],
                                        ALU.add).then_inc(hsum_s, 1)

            def sum_deltas(n):
                i0, i1 = POOL_DELTAS[0], POOL_DELTAS[n + 1]
                (s0, d0), (s1, d1) = delta(0, i0), delta(0, i1)
                pool.wait_ge(wq_scaled, n + 2)
                if n:
                    pool.wait_ge(pool_sum, n)
                nc.gpsimd.tensor_tensor(wqf[:, s0, d0, :], wqf[:, s0, d0, :], wqf[:, s1, d1, :],
                                        ALU.add).then_inc(pool_sum, 1)

            sum_halves(0)
            sum_deltas(0)
            sum_halves(1)
            sum_deltas(1)
            sum_deltas(2)
            for n in range(HALVES * KC):
                h, m = n // KC, n % KC
                pool.wait_ge(y_hi, n + 1)
                nc.gpsimd.tensor_tensor(act_lo[:, Y_SLOT[h], m, :], res[:, h, m, :],
                                        act_hi[:, Y_SLOT[h], m, :].bitcast(fp32),
                                        ALU.subtract).then_inc(y_lo, 1)

        @block.scalar
        def _(act):
            act.wait_ge(zeros_s, 1)
            nc.scalar.activation(tab[:, :], zeros[:, 0:1], ACT.Exp)

            def split_x(h, k):
                act.wait_ge(x_in[h][k], 16)
                nc.scalar.copy(act_hi[:, h, k, :], res[:, h, k, :]).then_inc(x_hi, 1)

            def evacuate(n):
                act.wait_ge(tile_mm, n + 1)
                nc.scalar.copy(hx[:, n, :, :],
                               bank[H_BANK[n]][:, 0:2 * AG].rearrange("p (t c) -> p t c", t=2)).then_inc(hx_out, 1)

            def shift_w1(q):
                act.wait_ge(w1_in[q], 16)
                act.wait_ge(shift_s, 1)
                nc.scalar.activation(w1[:, q, :], w1[:, q, :], ACT.Identity,
                                     bias=shift[:, 0:1]).then_inc(w1_shifted, 1)

            def scale_delta(i):
                s, d = delta(0, i)
                act.wait_ge(wq_in[i // 2], 16)
                nc.scalar.activation(wqf[:, s, d, :], wq[:, s, d, :], ACT.Copy,
                                     scale=wcoef[:, i:i + 1]).then_inc(wq_scaled, 1)

            def split_hgT(h):
                act.wait_ge(hgT_mm, h + 1)
                nc.scalar.copy(hgT_hi[:, h, :], bank[T_BANK][:, :]).then_inc(hgT_hi_s, 1)

            def split_y(n):
                h, m = n // KC, n % KC
                act.wait_ge(y_s, n + 1)
                nc.scalar.copy(act_hi[:, Y_SLOT[h], m, :], res[:, h, m, :]).then_inc(y_hi, 1)

            def split_w1(q):
                act.wait_ge(dw_i, DW_DONE[q])
                nc.scalar.copy(w1_hi[:, q, :], w1[:, q, :]).then_inc(w1_hi_s, 1)

            for k in range(KC):
                split_x(0, k)
            act.wait_ge(ag_in, 16)
            nc.scalar.copy(ag_hl[:, :, 0, :], ag[:, :, :]).then_inc(ag_hi_s, 1)
            shift_w1(0)
            for k in range(KC):
                split_x(1, k)
            for n in range(TPH):
                evacuate(n)
            scale_delta(2)
            evacuate(4)
            scale_delta(3)
            evacuate(5)
            act.wait_ge(be_in, 16)
            nc.scalar.copy(be_hi[:, :], be[:, :]).then_inc(be_hi_s, 1)
            evacuate(6)
            scale_delta(4)
            evacuate(7)
            act.wait_ge(gap_s, 1)
            nc.scalar.activation(eg[:, :], gap[:, :], ACT.Exp).then_inc(eg_s, 1)
            scale_delta(5)
            split_hgT(0)
            shift_w1(1)
            split_hgT(1)
            split_y(0)
            split_y(1)
            split_w1(0)
            for n in range(2, 2 * KC):
                split_y(n)
            split_w1(1)

        @block.vector
        def _(dve):
            steps = [0]

            def link(ins):
                steps[0] += 1
                ins.then_inc(dve_step, 1)
                dve.wait_ge(dve_step, steps[0])

            nc.vector.memset(zeros[:, :], 0.0).then_inc(zeros_s, 1)
            for k in range(KC):
                dve.wait_ge(w0_in[k], 16)
                nc.vector.tensor_copy(w0_hi[:, k, :], w0[:, k, :]).then_inc(w0_hi_s, 1)
                dve.wait_ge(w0_hi_s, k + 1)
                nc.vector.tensor_tensor(w0_lo[:, k, :], w0[:, k, :], w0_hi[:, k, :].bitcast(fp32),
                                        ALU.subtract).then_inc(w0_lo_s, 1)
            dve.wait_ge(sf_in, 16)
            dve.wait_ge(si_in, 16)
            nc.vector.tensor_tensor(wcoef[:, :], scale, wscale, ALU.mult)
            nc.vector.tensor_tensor(bcoef[:, :], scale, bscale, ALU.mult)
            link(nc.vector.tensor_tensor(slen[:, :], scale, length, ALU.mult))
            link(nc.vector.reduce_sum(shift[:, 0:1], slen[:, :], axis=AX.X))
            nc.vector.tensor_scalar(b1[:, :], bias_o, shift[:, 0:1], None, ALU.add).then_inc(shift_s, 1)
            dve.wait_ge(ag_hi_s, 1)
            nc.vector.tensor_tensor(ag_hl[:, :, 1, :], ag[:, :, :], ag_hl[:, :, 0, :].bitcast(fp32),
                                    ALU.subtract).then_inc(ag_lo_s, 1)
            link(nc.vector.tensor_tensor(bprod[:, :, :], bq,
                                         bcoef[:, :].unsqueeze(1).to_broadcast([P, KC, NW]), ALU.mult))
            link(nc.vector.reduce_sum(bsum[:, :], bprod[:, :, :], axis=AX.X))
            link(nc.vector.tensor_tensor(b1[:, :], b1[:, :], bsum[:, :], ALU.add))
            dve.wait_ge(lane_s, 1)
            link(nc.vector.tensor_tensor(lbias[:, :, :], lane[:, 0, :].unsqueeze(1).to_broadcast([P, TILES, E]),
                                         expert.unsqueeze(2).to_broadcast([P, TILES, E]), ALU.is_equal))
            link(nc.vector.tensor_scalar(lbias[:, :, :], lbias[:, :, :], LANG_BIAS, None, ALU.mult))

            adds = [0]

            def added(ins):
                adds[0] += 1
                ins.then_inc(dw_i, 1)

            def add_delta(q, i):
                s, d = delta(q, i)
                if i % 2 == 0:
                    dve.wait_ge(wq_in[q * QUADS + i // 2], 16)
                if i == 0:
                    dve.wait_ge(w1_shifted, q + 1)
                elif adds[0]:
                    dve.wait_ge(dw_i, adds[0])
                added(nc.vector.scalar_tensor_tensor(w1[:, q, :], wq[:, s, d, :], wcoef[:, i:i + 1],
                                                     w1[:, q, :], ALU.mult, ALU.add))

            def add_pool_sum():
                s, d = delta(0, POOL_DELTAS[0])
                dve.wait_ge(pool_sum, len(POOL_DELTAS) - 1)
                dve.wait_ge(dw_i, adds[0])
                added(nc.vector.tensor_tensor(w1[:, 0, :], w1[:, 0, :], wqf[:, s, d, :], ALU.add))

            def route():
                dve.wait_ge(hx_out, TILES)
                link(nc.vector.tensor_tensor(lg0[:, :, :], hx[:, :, 0, ER:AG], hx[:, :, 1, ER:AG], ALU.add))
                link(nc.vector.tensor_tensor(lg[:, :, :], lg0[:, :, :], lbias[:, :, :], ALU.add))
                for n in range(TILES):
                    last = nc.vector.max(top[:, n, :], lg[:, n, :])
                link(last)
                nc.vector.tensor_tensor(gap[:, :], top[:, :, 1], top[:, :, 0], ALU.subtract).then_inc(gap_s, 1)
                for n in range(TILES):
                    last = nc.vector.max_index(topi[:, n, :], top[:, n, :], lg[:, n, :])
                link(last)
                nc.vector.tensor_tensor(
                    hot[:, :, :, :], lane[:, :, :].unsqueeze(1).to_broadcast([P, TILES, TOP_K, E]),
                    topi[:, :, 0:TOP_K].unsqueeze(3).to_broadcast([P, TILES, TOP_K, E]), ALU.is_equal)
                dve.wait_ge(eg_s, 1)
                link(nc.vector.tensor_scalar(den[:, :], eg[:, :], 1.0, None, ALU.add))
                link(nc.vector.reciprocal(rden[:, :], den[:, :]))
                nc.vector.tensor_scalar(wts[:, :, 0], rden[:, :], SCALING, None, ALU.mult)
                link(nc.vector.scalar_tensor_tensor(wts[:, :, 1], eg[:, :], SCALING, rden[:, :],
                                                    ALU.mult, ALU.mult))
                link(nc.vector.tensor_tensor(hot[:, :, :, :], hot[:, :, :, :],
                                             wts[:, :, :].unsqueeze(3).to_broadcast([P, TILES, TOP_K, E]), ALU.mult))
                link(nc.vector.tensor_tensor(gates[:, :, :], hot[:, :, 0, :], hot[:, :, 1, :], ALU.add))

            def gate_h(h):
                ts = slice(h * TPH, (h + 1) * TPH)
                dve.wait_ge(hsum_s, h + 1)
                h4 = hg[:, ts, :].rearrange("p t (e r) -> p t e r", e=E)
                nc.vector.tensor_tensor(h4, h4, gates[:, ts, :].unsqueeze(3).to_broadcast([P, TPH, E, R]),
                                        ALU.mult).then_inc(hg_s, 1)

            def hgT_low(h):
                dve.wait_ge(hgT_hi_s, h + 1)
                nc.vector.tensor_tensor(hgT_lo[:, h, :], bank[T_BANK][:, :], hgT_hi[:, h, :].bitcast(fp32),
                                        ALU.subtract).then_inc(hgT_lo_s, 1)

            def add_residual(n):
                h, m = n // KC, n % KC
                dve.wait_ge(l0_mm, n + 1)
                nc.vector.tensor_tensor(res[:, h, m, :], bank[L0_BANK[h][m]][:, :], res[:, h, m, :],
                                        ALU.add).then_inc(y_s, 1)

            def w1_low(q):
                dve.wait_ge(w1_hi_s, q + 1)
                nc.vector.tensor_tensor(w1_lo[:, q, :], w1[:, q, :], w1_hi[:, q, :].bitcast(fp32),
                                        ALU.subtract).then_inc(w1_lo_s, 1)

            add_delta(0, 0)
            add_delta(0, 1)
            for k in range(KC):
                dve.wait_ge(x_hi, KC + k + 1)
                nc.vector.tensor_tensor(act_lo[:, 1, k, :], res[:, 1, k, :], act_hi[:, 1, k, :].bitcast(fp32),
                                        ALU.subtract).then_inc(x1_lo, 1)
            dve.wait_ge(be_hi_s, 1)
            nc.vector.tensor_tensor(be_lo[:, :], be[:, :], be_hi[:, :].bitcast(fp32), ALU.subtract).then_inc(be_lo_s, 1)
            route()
            gate_h(0)
            gate_h(1)
            add_delta(0, 6)
            hgT_low(0)
            add_delta(0, 7)
            add_pool_sum()
            hgT_low(1)
            add_residual(0)
            add_residual(1)
            add_delta(1, 0)
            add_residual(2)
            w1_low(0)
            add_residual(3)
            add_delta(1, 1)
            add_residual(4)
            add_delta(1, 2)
            add_residual(5)
            add_residual(6)
            add_delta(1, 3)
            add_residual(7)
            for i in range(4, NW):
                add_delta(1, i)
            w1_low(1)
            for n in range(HALVES * KC):
                h, o = n // KC, n % KC
                dve.wait_ge(l1_mm, n + 1)
                nc.vector.scalar_tensor_tensor(res[:, h, o, :], bank[L1_BANK[h][o]][:, :], b1[:, o:o + 1],
                                               res[:, h, o, :], ALU.add, ALU.add).then_inc(out_s, 1)

        @block.tensor
        def _(pe):
            def mm3(dst, w_hi, w_lo, a_hi, a_lo, first, last):
                nc.tensor.matmul(dst, w_hi, a_hi, start=first, stop=False)
                nc.tensor.matmul(dst, w_hi, a_lo, start=False, stop=False)
                return nc.tensor.matmul(dst, w_lo, a_hi, start=False, stop=last)

            def l0_step(h, m, k):
                mm3(bank[L0_BANK[h][m]][:, :], w0_hi[:, k, m * P:(m + 1) * P], w0_lo[:, k, m * P:(m + 1) * P],
                    act_hi[:, h, k, :], act_lo[:, h, k, :], k == 0, False)

            def lora_step(h, m):
                mm3(bank[L0_BANK[h][m]][:, :], be_hi[:, m * P:(m + 1) * P], be_lo[:, m * P:(m + 1) * P],
                    hgT_hi[:, h, :], hgT_lo[:, h, :], False, True).then_inc(l0_mm, 1)

            def experts(n):
                if n >= H_BANKS:
                    pe.wait_ge(hx_out, n - H_BANKS + 1)
                h, c = n // TPH, (n % TPH) * P
                for k in range(KC):
                    nc.tensor.matmul(bank[H_BANK[n]][:, 0:2 * AG], act_hi[:, h, k, c:c + P],
                                     ag_hl[:, k, :, :].rearrange("p t c -> p (t c)"), start=k == 0, stop=False)
                    last = nc.tensor.matmul(bank[H_BANK[n]][:, 0:AG], act_lo[:, h, k, c:c + P],
                                            ag_hl[:, k, 0, :], start=False, stop=k == KC - 1)
                last.then_inc(tile_mm, 1)

            def transpose_hg(h):
                pe.wait_ge(hg_s, h + 1)
                for j in range(TPH):
                    last = nc.tensor.transpose(bank[T_BANK][:, j * P:(j + 1) * P], hg[:, h * TPH + j, :], ident[:, :])
                last.then_inc(hgT_mm, 1)

            def l1_step(h, o, k):
                s, c = Y_SLOT[h], (k % 2) * D + o * P
                return mm3(bank[L1_BANK[h][o]][:, :], w1_hi[:, k // 2, c:c + P], w1_lo[:, k // 2, c:c + P],
                           act_hi[:, s, k, :], act_lo[:, s, k, :], k == 0, k == KC - 1)

            pe.wait_ge(zeros_s, 1)
            for _ in range(WARM):
                nc.tensor.matmul(bank[T_BANK][:, :], zeros[:, 0:P], zeros[:, :], start=True, stop=True)
            pe.wait_ge(w0_hi_s, 1)
            pe.wait_ge(x_hi, 1)
            for m in range(KC):
                nc.tensor.matmul(bank[L0_BANK[0][m]][:, :], w0_hi[:, 0, m * P:(m + 1) * P], act_hi[:, 0, 0, :],
                                 start=True, stop=False)
            pe.wait_ge(w0_lo_s, 1)
            for m in range(KC):
                nc.tensor.matmul(bank[L0_BANK[0][m]][:, :], w0_lo[:, 0, m * P:(m + 1) * P], act_hi[:, 0, 0, :],
                                 start=False, stop=False)
            pe.wait_ge(x0_lo, 1)
            for m in range(KC):
                nc.tensor.matmul(bank[L0_BANK[0][m]][:, :], w0_hi[:, 0, m * P:(m + 1) * P], act_lo[:, 0, 0, :],
                                 start=False, stop=False)
            for k in range(1, KC):
                pe.wait_ge(w0_lo_s, k + 1)
                pe.wait_ge(x0_lo, k + 1)
                for m in range(KC):
                    l0_step(0, m, k)
            pe.wait_ge(ag_lo_s, 1)
            for n in range(TPH):
                experts(n)
            pe.wait_ge(x1_lo, KC)
            for n in range(TPH, TILES):
                experts(n)
            pe.wait_ge(hx_out, TILES - 2)
            for k in range(KC):
                l0_step(1, 0, k)
            pe.wait_ge(hx_out, TILES - 1)
            for k in range(KC):
                l0_step(1, 1, k)
            pe.wait_ge(ident_s, 1)
            transpose_hg(0)
            pe.wait_ge(hx_out, TILES)
            for k in range(KC):
                l0_step(1, 2, k)
            pe.wait_ge(hgT_lo_s, 1)
            transpose_hg(1)
            pe.wait_ge(be_lo_s, 1)
            for m in range(KC):
                lora_step(0, m)
            pe.wait_ge(hgT_lo_s, 2)
            for m in range(KC - 1):
                lora_step(1, m)
            pe.wait_ge(y_s, 1)
            for k in range(KC):
                l0_step(1, KC - 1, k)
            lora_step(1, KC - 1)
            pe.wait_ge(w1_lo_s, 1)
            for h in range(HALVES):
                pe.wait_ge(y_lo, (h + 1) * KC)
                for o in range(KC):
                    for k in range(2):
                        l1_step(h, o, k)
            pe.wait_ge(w1_lo_s, 2)
            for h in range(HALVES):
                for o in range(KC):
                    l1_step(h, o, 2)
                    l1_step(h, o, 3).then_inc(l1_mm, 1)


def kernel(x, itok_B_0_7, condB_scale, itok_Bx4096x4096_0_255, condB_wscale, itok_Bx4096_0_255, condB_bscale,
           _lenS, L0_cond_W, L0_cond_Wr, L0_cond_A, L0_cond_B, L1_cond_weight, L1_cond_bias):
    import numpy as np
    import concourse.bacc as bacc
    from concourse import mybir as mb
    from concourse.bass_utils import run_bass_kernel_spmd

    def rows_on_partitions(m):
        return np.asarray(m).reshape(KC, P, -1).transpose(1, 0, 2)

    def every_partition(v):
        return np.broadcast_to(np.asarray(v), (P, NW))

    x = np.asarray(x)
    ag = np.concatenate([np.asarray(L0_cond_A).reshape(ER, D), np.asarray(L0_cond_Wr)], axis=0)
    wq = np.asarray(itok_Bx4096x4096_0_255)
    arrays = {
        "x_t": x.reshape(HALVES, TH, KC, P).transpose(3, 0, 2, 1),
        "w0_t": rows_on_partitions(np.asarray(L0_cond_W).T),
        "ag_t": rows_on_partitions(ag.T),
        "b_er": np.asarray(L0_cond_B).transpose(0, 2, 1).reshape(ER, D),
        "w1_t": rows_on_partitions(np.asarray(L1_cond_weight).T).reshape(P, PAIRS, PD),
        "wq_t": wq.transpose(2, 0, 1).reshape(PAIRS, 2, P, NW, D).transpose(2, 0, 3, 1, 4).reshape(P, PAIRS, NW, PD),
        "small_f": np.concatenate([every_partition(condB_scale), every_partition(condB_wscale),
                                   every_partition(condB_bscale), np.asarray(L1_cond_bias).reshape(KC, P).T], axis=1),
        "small_i": np.concatenate([every_partition(itok_B_0_7), every_partition(_lenS),
                                   np.asarray(itok_Bx4096_0_255).reshape(NW, KC, P).transpose(2, 1, 0).reshape(P, -1)],
                                  axis=1),
    }
    nc = bacc.Bacc("TRN2", target_bir_lowering=False, num_devices=1)
    args = []
    for name in arrays:
        arrays[name] = np.ascontiguousarray(arrays[name])
        a = arrays[name]
        args.append(nc.dram_tensor(name, a.shape, mb.dt.from_np(a.dtype), kind="ExternalInput").ap())
    out = nc.dram_tensor("out_t", (P, HALVES, KC, TH), mb.dt.float32, kind="ExternalOutput").ap()
    cond_resid_kernel(nc, *args, out)
    r = run_bass_kernel_spmd(nc, [arrays], core_ids=[0])
    out_t = r.results[0]["out_t"]
    return out_t.transpose(1, 3, 2, 0).reshape(BATCH, SEQ, D)
```

```python
import concourse.bass as bass
from concourse import mybir
from contextlib import ExitStack


P = 128
BATCH = 8
SEQ = 128
D = 512
E = 8
R = 16
NW = 8
TOP_K = 2
LANG_BIAS = 5.0
SCALING = 2.0
KC = D // P
TOK = BATCH * SEQ
HALVES = 2
TH = TOK // HALVES
TILES = TOK // P
TPH = TILES // HALVES
ER = E * R
AG = ER + E
PAIRS = KC // 2
PD = 2 * D
QUADS = NW // 2
WQ_PIECES = PAIRS * QUADS
WQ_SLOTS = 6
H_BANKS = 3
WARM = 8


def cond_resid_kernel(nc, x_t, w0_t, ag_t, b_er, w1_t, wq_t, small_f, small_i, out_t):
    fp32 = mybir.dt.float32
    f32r = mybir.dt.float32r
    bf16 = mybir.dt.bfloat16
    i32 = mybir.dt.int32
    u32 = mybir.dt.uint32
    ALU = mybir.AluOpType
    ACT = mybir.ActivationFunctionType
    AX = mybir.AxisListType

    ctx = ExitStack()
    with ctx:
        def sb(name, shape, dt=fp32):
            return ctx.enter_context(nc.sbuf_tensor(name, shape, dt))

        def sem(name):
            return ctx.enter_context(nc.semaphore(name))

        xo = sb("xo", [P, HALVES, KC, TH])
        act_hi = sb("act_hi", [P, 3, KC, TH], f32r)
        act_lo = sb("act_lo", [P, 3, KC, TH], f32r)
        Y_SLOT = [2, 0]
        w0 = sb("w0", [P, KC, D])
        w0_hi = sb("w0_hi", [P, KC, D], f32r)
        w0_lo = sb("w0_lo", [P, KC, D], f32r)
        ag = sb("ag", [P, KC, AG])
        ag_hl = sb("ag_hl", [P, KC, 2, AG], f32r)
        be = sb("be", [P, D])
        be_hi = sb("be_hi", [P, D], f32r)
        be_lo = sb("be_lo", [P, D], f32r)
        w1 = sb("w1", [P, PAIRS, PD])
        w1_hi = sb("w1_hi", [P, PAIRS, PD], f32r)
        w1_lo = sb("w1_lo", [P, PAIRS, PD], f32r)
        wq = sb("wq", [P, WQ_SLOTS, 2, PD], i32)
        wqf = wq[:, :, :, :].bitcast(fp32)
        hx = sb("hx", [P, TILES, 2, AG])
        hg = sb("hg", [P, TILES, ER])
        hgT_hi = sb("hgT_hi", [P, HALVES, TH], f32r)
        hgT_lo = sb("hgT_lo", [P, HALVES, TH], f32r)
        sf = sb("sf", [P, 3 * NW + KC])
        scale, wscale, bscale = (sf[:, i * NW:(i + 1) * NW] for i in range(3))
        bias_o = sf[:, 3 * NW:3 * NW + KC]
        si = sb("si", [P, 2 * NW + KC * NW], i32)
        expert = si[:, 0:NW]
        length = si[:, NW:2 * NW]
        bq = si[:, 2 * NW:2 * NW + KC * NW].rearrange("p (k i) -> p k i", k=KC)
        wcoef = sb("wcoef", [P, NW])
        bcoef = sb("bcoef", [P, NW])
        slen = sb("slen", [P, NW])
        shift = sb("shift", [P, 1])
        bprod = sb("bprod", [P, KC, NW])
        bsum = sb("bsum", [P, KC])
        b1 = sb("b1", [P, KC])
        lane = sb("lane", [P, TOP_K, E])
        lbias = sb("lbias", [P, TILES, E])
        lg0 = sb("lg0", [P, TILES, E])
        lg = sb("lg", [P, TILES, E])
        top = sb("top", [P, TILES, 8])
        topi = sb("topi", [P, TILES, 8], u32)
        gap = sb("gap", [P, TILES])
        eg = sb("eg", [P, TILES])
        den = sb("den", [P, TILES])
        rden = sb("rden", [P, TILES])
        wts = sb("wts", [P, TILES, TOP_K])
        hot = sb("hot", [P, TILES, TOP_K, E])
        gates = sb("gates", [P, TILES, E])
        ident = sb("ident", [P, P])
        zeros = sb("zeros", [P, TH], bf16)
        tab = sb("tab", [P, 1])

        bank = [ctx.enter_context(nc.psum_tensor(f"bank{i}", [P, TH], fp32)) for i in range(8)]
        L0_BANK = [[0, 1, 2, 3], [6, 4, 5, 0]]
        H_BANK = [4 + n % H_BANKS for n in range(TILES)]
        T_BANK = 7
        L1_BANK = [[1, 2, 3, 7], [6, 4, 5]]
        LAST_BANK = [1, 2]

        LAST_PIECE = HALVES * KC - 1
        OUT_PIECES = [(n // KC, n % KC, slice(0, TH)) for n in range(LAST_PIECE)]
        OUT_PIECES += [(HALVES - 1, KC - 1, slice(c, c + TH // 2)) for c in (0, TH // 2)]

        x_in = [[sem(f"x_in{h}{k}") for k in range(KC)] for h in range(HALVES)]
        w0_first_in = sem("w0_first_in")
        w0_in = [sem(f"w0_in{k}") for k in range(KC)]
        ag_in = sem("ag_in")
        be_in = sem("be_in")
        w1_in = [sem(f"w1_in{q}") for q in range(PAIRS)]
        wq_in = [sem(f"wq_in{j}") for j in range(WQ_PIECES)]
        sf_in = sem("sf_in")
        si_in = sem("si_in")
        out_stored = sem("out_stored")
        x_hi = sem("x_hi")
        ag_hi_s = sem("ag_hi_s")
        be_hi_s = sem("be_hi_s")
        w1_shifted = sem("w1_shifted")
        w1_hi_s = sem("w1_hi_s")
        wq_scaled = sem("wq_scaled")
        hx_out = sem("hx_out")
        eg_s = sem("eg_s")
        hgT_hi_s = sem("hgT_hi_s")
        y_hi = sem("y_hi")
        out_s = sem("out_s")
        zeros_s = sem("zeros_s")
        w0_diag = sem("w0_diag")
        w0_first_hi = sem("w0_first_hi")
        w0_hi_s = sem("w0_hi_s")
        w0_lo_s = sem("w0_lo_s")
        x_lo = sem("x_lo")
        ag_lo_s = sem("ag_lo_s")
        shift_s = sem("shift_s")
        gap_s = sem("gap_s")
        hg_s = sem("hg_s")
        hgT_lo_s = sem("hgT_lo_s")
        y_lo = sem("y_lo")
        dw = [sem(f"dw{q}") for q in range(PAIRS)]
        w1_lo1_s = sem("w1_lo1_s")
        dve_step = sem("dve_step")
        lane_s = sem("lane_s")
        ident0 = sem("ident0")
        ident_s = sem("ident_s")
        hsum_s = sem("hsum_s")
        be_lo_s = sem("be_lo_s")
        pool_sum = sem("pool_sum")
        w1_lo0_s = sem("w1_lo0_s")
        tile_mm = sem("tile_mm")
        l0_mm = sem("l0_mm")
        hgT_mm = sem("hgT_mm")
        l1_mm = sem("l1_mm")

        POOL_DELTAS = [(4, 5, 6, 7), (2, 3)]
        DW_TERMS = [NW - len(p) + 1 for p in POOL_DELTAS]

        def wqf_of(q, i):
            return wqf[:, (q * QUADS + i // 2) % WQ_SLOTS, i % 2, :]

        block = ctx.enter_context(nc.Block())

        @block.sync
        def _(sp):
            def load_wq(j):
                if j >= WQ_SLOTS:
                    sp.wait_ge(dw[0], 2 * (j - WQ_SLOTS + 1))
                q, d = j // QUADS, 2 * (j % QUADS)
                sp.dma_start(wq[:, j % WQ_SLOTS, :, :], wq_t[:, q, d:d + 2, :]).then_inc(wq_in[j], 16)

            for k in range(KC):
                sp.dma_start(xo[:, 0, k, :], x_t[:, 0, k, :]).then_inc(x_in[0][k], 16)
                if k == 0:
                    sp.dma_start(w0[:, 0, P:D], w0_t[:, 0, P:D]).then_inc(w0_first_in, 16)
                    sp.dma_start(w0[:, 0, 0:P], w0_t[:, 0, 0:P]).then_inc(w0_in[0], 16)
                else:
                    sp.dma_start(w0[:, k, :], w0_t[:, k, :]).then_inc(w0_in[k], 16)
            sp.dma_start(ag[:, :, :], ag_t).then_inc(ag_in, 16)
            sp.dma_start(sf[:, :], small_f).then_inc(sf_in, 16)
            sp.dma_start(si[:, :], small_i).then_inc(si_in, 16)
            sp.dma_start(w1[:, 0, :], w1_t[:, 0, :]).then_inc(w1_in[0], 16)
            load_wq(0)
            for k in range(KC):
                sp.dma_start(xo[:, 1, k, :], x_t[:, 1, k, :]).then_inc(x_in[1][k], 16)
            load_wq(1)
            sp.dma_start(be[:, :], b_er).then_inc(be_in, 16)
            load_wq(2)
            load_wq(3)
            sp.dma_start(w1[:, 1, :], w1_t[:, 1, :]).then_inc(w1_in[1], 16)
            for j in range(QUADS, WQ_PIECES):
                load_wq(j)
            for n, (h, o, c) in enumerate(OUT_PIECES):
                sp.wait_ge(out_s, n + 1)
                sp.dma_start(out_t[:, h, o, c], xo[:, h, o, c]).then_inc(out_stored, 16)
            sp.wait_ge(out_stored, 16 * len(OUT_PIECES))

        @block.gpsimd
        def _(pool):
            nc.gpsimd.memset(ident[:, :], 0.0).then_inc(ident0, 1)
            nc.gpsimd.iota(lane[:, :, :], pattern=[[0, TOP_K], [1, E]], base=0, channel_multiplier=0,
                           allow_small_or_imprecise_dtypes=True).then_inc(lane_s, 1)
            pool.wait_ge(ident0, 1)
            nc.gpsimd.affine_select(out=ident[:, :], in_=ident[:, :], compare_op=ALU.not_equal, fill=1.0,
                                    base=0, pattern=[[-1, P]], channel_multiplier=1).then_inc(ident_s, 1)

            def sum_halves(h):
                ts = slice(h * TPH, (h + 1) * TPH)
                pool.wait_ge(hx_out, TPH * (h + 1))
                nc.gpsimd.tensor_tensor(hg[:, ts, :], hx[:, ts, 0, 0:ER], hx[:, ts, 1, 0:ER],
                                        ALU.add).then_inc(hsum_s, 1)

            scaled, added = [0], [0]

            def sum_up(q):
                for n in range(1, len(POOL_DELTAS[q])):
                    total, term = wqf_of(q, POOL_DELTAS[q][0]), wqf_of(q, POOL_DELTAS[q][n])
                    pool.wait_ge(wq_scaled, scaled[0] + n + 1)
                    if n > 1:
                        pool.wait_ge(pool_sum, added[0])
                    nc.gpsimd.tensor_tensor(total, total, term, ALU.add).then_inc(pool_sum, 1)
                    added[0] += 1
                scaled[0] += len(POOL_DELTAS[q])

            def w1_low(k):
                c = slice(k * D, (k + 1) * D)
                pool.wait_ge(w1_hi_s, k + 1)
                nc.gpsimd.tensor_tensor(w1_lo[:, 0, c], w1[:, 0, c], w1_hi[:, 0, c].bitcast(fp32),
                                        ALU.subtract).then_inc(w1_lo0_s, 1)

            sum_halves(0)
            pool.wait_ge(be_hi_s, 1)
            nc.gpsimd.tensor_tensor(be_lo[:, :], be[:, :], be_hi[:, :].bitcast(fp32),
                                    ALU.subtract).then_inc(be_lo_s, 1)
            sum_halves(1)
            for q in range(PAIRS):
                sum_up(q)
            w1_low(0)
            w1_low(1)

        @block.scalar
        def _(act):
            act.wait_ge(zeros_s, 1)
            nc.scalar.activation(tab[:, :], zeros[:, 0:1], ACT.Exp)

            def split_x(h, k):
                act.wait_ge(x_in[h][k], 16)
                nc.scalar.copy(act_hi[:, h, k, :], xo[:, h, k, :]).then_inc(x_hi, 1)

            def evacuate(n):
                act.wait_ge(tile_mm, n + 1)
                nc.scalar.copy(hx[:, n, :, :],
                               bank[H_BANK[n]][:, 0:2 * AG].rearrange("p (t c) -> p t c", t=2)).then_inc(hx_out, 1)

            def shift_w1(q):
                act.wait_ge(w1_in[q], 16)
                act.wait_ge(shift_s, 1)
                nc.scalar.activation(w1[:, q, :], w1[:, q, :], ACT.Identity,
                                     bias=shift[:, 0:1]).then_inc(w1_shifted, 1)

            def split_hgT(h):
                act.wait_ge(hgT_mm, h + 1)
                nc.scalar.copy(hgT_hi[:, h, :], bank[T_BANK][:, :]).then_inc(hgT_hi_s, 1)

            def split_y(n):
                h, m = n // KC, n % KC
                act.wait_ge(l0_mm, n + 1)
                nc.scalar.copy(act_hi[:, Y_SLOT[h], m, :], bank[L0_BANK[h][m]][:, :]).then_inc(y_hi, 1)

            def scale_delta(q, i):
                j = q * QUADS + i // 2
                act.wait_ge(wq_in[j], 16)
                nc.scalar.activation(wqf_of(q, i), wq[:, j % WQ_SLOTS, i % 2, :], ACT.Copy,
                                     scale=wcoef[:, i:i + 1]).then_inc(wq_scaled, 1)

            def split_w1(k):
                act.wait_ge(dw[k // 2], DW_TERMS[k // 2])
                nc.scalar.copy(w1_hi[:, k // 2, (k % 2) * D:(k % 2 + 1) * D],
                               w1[:, k // 2, (k % 2) * D:(k % 2 + 1) * D]).then_inc(w1_hi_s, 1)

            for k in range(KC):
                split_x(0, k)
            act.wait_ge(ag_in, 16)
            nc.scalar.copy(ag_hl[:, :, 0, :], ag[:, :, :]).then_inc(ag_hi_s, 1)
            shift_w1(0)
            for k in range(KC):
                split_x(1, k)
            for n in range(TPH):
                evacuate(n)
            act.wait_ge(be_in, 16)
            nc.scalar.copy(be_hi[:, :], be[:, :]).then_inc(be_hi_s, 1)
            evacuate(TPH)
            act.wait_ge(gap_s, 1)
            nc.scalar.activation(eg[:, 0:TPH], gap[:, 0:TPH], ACT.Exp).then_inc(eg_s, 1)
            for n in range(TPH + 1, TILES):
                evacuate(n)
            scale_delta(0, 4)
            scale_delta(0, 5)
            split_hgT(0)
            act.wait_ge(gap_s, 2)
            nc.scalar.activation(eg[:, TPH:TILES], gap[:, TPH:TILES], ACT.Exp).then_inc(eg_s, 1)
            shift_w1(1)
            scale_delta(0, 6)
            scale_delta(0, 7)
            split_y(0)
            split_y(1)
            split_hgT(1)
            split_y(2)
            split_y(3)
            scale_delta(1, 2)
            scale_delta(1, 3)
            split_w1(0)
            split_w1(1)
            for n in range(KC, 2 * KC):
                split_y(n)
            split_w1(2)
            split_w1(3)
            for n, (h, o, c) in enumerate(OUT_PIECES):
                act.wait_ge(l1_mm, n + 1)
                b = L1_BANK[h][o] if n < LAST_PIECE else LAST_BANK[n - LAST_PIECE]
                nc.scalar.activation(xo[:, h, o, c], bank[b][:, 0:c.stop - c.start], ACT.Identity,
                                     bias=b1[:, o:o + 1]).then_inc(out_s, 1)

        @block.vector
        def _(dve):
            steps = [0]

            def link(ins):
                steps[0] += 1
                ins.then_inc(dve_step, 1)
                dve.wait_ge(dve_step, steps[0])

            def x_low(h, k):
                dve.wait_ge(x_hi, KC * h + k + 1)
                nc.vector.tensor_tensor(act_lo[:, h, k, :], xo[:, h, k, :], act_hi[:, h, k, :].bitcast(fp32),
                                        ALU.subtract).then_inc(x_lo, 1)

            nc.vector.memset(zeros[:, :], 0.0).then_inc(zeros_s, 1)
            dve.wait_ge(w0_first_in, 16)
            nc.vector.tensor_copy(w0_hi[:, 0, P:D], w0[:, 0, P:D]).then_inc(w0_first_hi, 1)
            for k in range(KC):
                dve.wait_ge(w0_in[k], 16)
                if k == 0:
                    dve.wait_ge(ident_s, 1)
                dg = w0[:, k, k * P:(k + 1) * P]
                nc.vector.tensor_tensor(dg, dg, ident[:, :], ALU.add).then_inc(w0_diag, 1)
                dve.wait_ge(w0_diag, k + 1)
                if k == 0:
                    nc.vector.tensor_copy(w0_hi[:, 0, 0:P], w0[:, 0, 0:P]).then_inc(w0_hi_s, 1)
                    dve.wait_ge(w0_first_hi, 1)
                else:
                    nc.vector.tensor_copy(w0_hi[:, k, :], w0[:, k, :]).then_inc(w0_hi_s, 1)
                dve.wait_ge(w0_hi_s, k + 1)
                nc.vector.tensor_tensor(w0_lo[:, k, :], w0[:, k, :], w0_hi[:, k, :].bitcast(fp32),
                                        ALU.subtract).then_inc(w0_lo_s, 1)
                x_low(0, k)
            dve.wait_ge(sf_in, 16)
            dve.wait_ge(si_in, 16)
            nc.vector.tensor_tensor(wcoef[:, :], scale, wscale, ALU.mult)
            nc.vector.tensor_tensor(bcoef[:, :], scale, bscale, ALU.mult)
            link(nc.vector.tensor_tensor(slen[:, :], scale, length, ALU.mult))
            link(nc.vector.reduce_sum(shift[:, 0:1], slen[:, :], axis=AX.X))
            nc.vector.tensor_scalar(b1[:, :], bias_o, shift[:, 0:1], None, ALU.add).then_inc(shift_s, 1)
            dve.wait_ge(ag_hi_s, 1)
            nc.vector.tensor_tensor(ag_hl[:, :, 1, :], ag[:, :, :], ag_hl[:, :, 0, :].bitcast(fp32),
                                    ALU.subtract).then_inc(ag_lo_s, 1)
            link(nc.vector.tensor_tensor(bprod[:, :, :], bq,
                                         bcoef[:, :].unsqueeze(1).to_broadcast([P, KC, NW]), ALU.mult))
            link(nc.vector.reduce_sum(bsum[:, :], bprod[:, :, :], axis=AX.X))
            link(nc.vector.tensor_tensor(b1[:, :], b1[:, :], bsum[:, :], ALU.add))
            dve.wait_ge(lane_s, 1)
            link(nc.vector.tensor_tensor(lbias[:, :, :], lane[:, 0, :].unsqueeze(1).to_broadcast([P, TILES, E]),
                                         expert.unsqueeze(2).to_broadcast([P, TILES, E]), ALU.is_equal))
            link(nc.vector.tensor_scalar(lbias[:, :, :], lbias[:, :, :], LANG_BIAS, None, ALU.mult))

            def add_identity(q):
                dve.wait_ge(w1_shifted, q + 1)
                for j in range(2):
                    c = j * D + (2 * q + j) * P
                    last = nc.vector.tensor_tensor(w1[:, q, c:c + P], w1[:, q, c:c + P], ident[:, :], ALU.add)
                link(last)

            terms = [0, 0]

            def add_delta(q, i):
                j = q * QUADS + i // 2
                dve.wait_ge(wq_in[j], 16)
                if terms[q]:
                    dve.wait_ge(dw[q], terms[q])
                nc.vector.scalar_tensor_tensor(w1[:, q, :], wq[:, j % WQ_SLOTS, i % 2, :], wcoef[:, i:i + 1],
                                               w1[:, q, :], ALU.mult, ALU.add).then_inc(dw[q], 1)
                terms[q] += 1

            def add_pool_sum(q):
                dve.wait_ge(pool_sum, sum(len(p) - 1 for p in POOL_DELTAS[:q + 1]))
                dve.wait_ge(dw[q], terms[q])
                nc.vector.tensor_tensor(w1[:, q, :], w1[:, q, :], wqf_of(q, POOL_DELTAS[q][0]),
                                        ALU.add).then_inc(dw[q], 1)
                terms[q] += 1

            def route(h, meanwhile):
                ts = slice(h * TPH, (h + 1) * TPH)
                dve.wait_ge(hx_out, TPH * (h + 1))
                link(nc.vector.tensor_tensor(lg0[:, ts, :], hx[:, ts, 0, ER:AG], hx[:, ts, 1, ER:AG], ALU.add))
                link(nc.vector.tensor_tensor(lg[:, ts, :], lg0[:, ts, :], lbias[:, ts, :], ALU.add))
                for n in range(h * TPH, (h + 1) * TPH):
                    last = nc.vector.max(top[:, n, :], lg[:, n, :])
                link(last)
                nc.vector.tensor_tensor(gap[:, ts], top[:, ts, 1], top[:, ts, 0], ALU.subtract).then_inc(gap_s, 1)
                for n in range(h * TPH, (h + 1) * TPH):
                    last = nc.vector.max_index(topi[:, n, :], top[:, n, :], lg[:, n, :])
                link(last)
                meanwhile()
                nc.vector.tensor_tensor(
                    hot[:, ts, :, :], lane[:, :, :].unsqueeze(1).to_broadcast([P, TPH, TOP_K, E]),
                    topi[:, ts, 0:TOP_K].unsqueeze(3).to_broadcast([P, TPH, TOP_K, E]), ALU.is_equal)
                dve.wait_ge(eg_s, h + 1)
                link(nc.vector.tensor_scalar(den[:, ts], eg[:, ts], 1.0, None, ALU.add))
                link(nc.vector.reciprocal(rden[:, ts], den[:, ts]))
                nc.vector.tensor_scalar(wts[:, ts, 0], rden[:, ts], SCALING, None, ALU.mult)
                link(nc.vector.scalar_tensor_tensor(wts[:, ts, 1], eg[:, ts], SCALING, rden[:, ts],
                                                    ALU.mult, ALU.mult))
                link(nc.vector.tensor_tensor(hot[:, ts, :, :], hot[:, ts, :, :],
                                             wts[:, ts, :].unsqueeze(3).to_broadcast([P, TPH, TOP_K, E]), ALU.mult))
                link(nc.vector.tensor_tensor(gates[:, ts, :], hot[:, ts, 0, :], hot[:, ts, 1, :], ALU.add))
                dve.wait_ge(hsum_s, h + 1)
                h4 = hg[:, ts, :].rearrange("p t (e r) -> p t e r", e=E)
                nc.vector.tensor_tensor(h4, h4, gates[:, ts, :].unsqueeze(3).to_broadcast([P, TPH, E, R]),
                                        ALU.mult).then_inc(hg_s, 1)

            def hgT_low(h):
                dve.wait_ge(hgT_hi_s, h + 1)
                nc.vector.tensor_tensor(hgT_lo[:, h, :], bank[T_BANK][:, :], hgT_hi[:, h, :].bitcast(fp32),
                                        ALU.subtract).then_inc(hgT_lo_s, 1)

            def y_low(n):
                h, m = n // KC, n % KC
                dve.wait_ge(y_hi, n + 1)
                nc.vector.tensor_tensor(act_lo[:, Y_SLOT[h], m, :], bank[L0_BANK[h][m]][:, :],
                                        act_hi[:, Y_SLOT[h], m, :].bitcast(fp32), ALU.subtract).then_inc(y_lo, 1)

            def w1_low(k):
                c = slice((k % 2) * D, (k % 2 + 1) * D)
                dve.wait_ge(w1_hi_s, k + 1)
                nc.vector.tensor_tensor(w1_lo[:, 1, c], w1[:, 1, c], w1_hi[:, 1, c].bitcast(fp32),
                                        ALU.subtract).then_inc(w1_lo1_s, 1)

            add_identity(0)
            add_delta(0, 0)
            for k in range(KC):
                x_low(1, k)
            add_delta(0, 1)
            add_delta(0, 2)
            route(0, lambda: add_delta(0, 3))
            route(1, lambda: hgT_low(0))
            add_identity(1)
            add_delta(1, 0)
            add_delta(1, 1)
            y_low(0)
            hgT_low(1)
            y_low(1)
            add_pool_sum(0)
            y_low(2)
            y_low(3)
            add_delta(1, 4)
            add_delta(1, 5)
            add_pool_sum(1)
            y_low(4)
            y_low(5)
            y_low(6)
            add_delta(1, 6)
            y_low(7)
            add_delta(1, 7)
            w1_low(2)
            w1_low(3)

        @block.tensor
        def _(pe):
            def mm3(dst, w_hi, w_lo, a_hi, a_lo, first, last):
                nc.tensor.matmul(dst, w_hi, a_hi, start=first, stop=False)
                nc.tensor.matmul(dst, w_hi, a_lo, start=False, stop=False)
                return nc.tensor.matmul(dst, w_lo, a_hi, start=False, stop=last)

            def l0_step(h, m, k):
                mm3(bank[L0_BANK[h][m]][:, :], w0_hi[:, k, m * P:(m + 1) * P], w0_lo[:, k, m * P:(m + 1) * P],
                    act_hi[:, h, k, :], act_lo[:, h, k, :], k == 0, False)

            def lora_step(h, m):
                mm3(bank[L0_BANK[h][m]][:, :], be_hi[:, m * P:(m + 1) * P], be_lo[:, m * P:(m + 1) * P],
                    hgT_hi[:, h, :], hgT_lo[:, h, :], False, True).then_inc(l0_mm, 1)

            def experts(n):
                if n >= H_BANKS:
                    pe.wait_ge(hx_out, n - H_BANKS + 1)
                h, c = n // TPH, (n % TPH) * P
                for k in range(KC):
                    nc.tensor.matmul(bank[H_BANK[n]][:, 0:2 * AG], act_hi[:, h, k, c:c + P],
                                     ag_hl[:, k, :, :].rearrange("p t c -> p (t c)"), start=k == 0, stop=False)
                    last = nc.tensor.matmul(bank[H_BANK[n]][:, 0:AG], act_lo[:, h, k, c:c + P],
                                            ag_hl[:, k, 0, :], start=False, stop=k == KC - 1)
                last.then_inc(tile_mm, 1)

            def transpose_hg(h):
                pe.wait_ge(hg_s, h + 1)
                for j in range(TPH):
                    last = nc.tensor.transpose(bank[T_BANK][:, j * P:(j + 1) * P], hg[:, h * TPH + j, :], ident[:, :])
                last.then_inc(hgT_mm, 1)

            def l1_step(b, h, o, k, c=slice(0, TH)):
                s, w = Y_SLOT[h], (k % 2) * D + o * P
                return mm3(bank[b][:, 0:c.stop - c.start], w1_hi[:, k // 2, w:w + P], w1_lo[:, k // 2, w:w + P],
                           act_hi[:, s, k, c], act_lo[:, s, k, c], k == 0, k == KC - 1)

            pe.wait_ge(zeros_s, 1)
            for _ in range(WARM):
                nc.tensor.matmul(bank[T_BANK][:, :], zeros[:, 0:P], zeros[:, :], start=True, stop=True)
            pe.wait_ge(w0_first_hi, 1)
            pe.wait_ge(x_hi, 1)
            for m in list(range(1, KC)) + [0]:
                if m == 0:
                    pe.wait_ge(w0_hi_s, 1)
                nc.tensor.matmul(bank[L0_BANK[0][m]][:, :], w0_hi[:, 0, m * P:(m + 1) * P], act_hi[:, 0, 0, :],
                                 start=True, stop=False)
            pe.wait_ge(w0_lo_s, 1)
            for m in range(KC):
                nc.tensor.matmul(bank[L0_BANK[0][m]][:, :], w0_lo[:, 0, m * P:(m + 1) * P], act_hi[:, 0, 0, :],
                                 start=False, stop=False)
            pe.wait_ge(x_lo, 1)
            for m in range(KC):
                nc.tensor.matmul(bank[L0_BANK[0][m]][:, :], w0_hi[:, 0, m * P:(m + 1) * P], act_lo[:, 0, 0, :],
                                 start=False, stop=False)
            for k in range(1, KC):
                pe.wait_ge(w0_lo_s, k + 1)
                pe.wait_ge(x_lo, k + 1)
                for m in range(KC):
                    l0_step(0, m, k)
            pe.wait_ge(ag_lo_s, 1)
            for n in range(TPH):
                experts(n)
            pe.wait_ge(x_lo, 2 * KC)
            for n in range(TPH, TILES):
                experts(n)
            pe.wait_ge(hx_out, TILES - 2)
            for k in range(KC):
                l0_step(1, 0, k)
            pe.wait_ge(ident_s, 1)
            transpose_hg(0)
            pe.wait_ge(hx_out, TILES - 1)
            for k in range(KC):
                l0_step(1, 1, k)
            pe.wait_ge(hgT_lo_s, 1)
            pe.wait_ge(be_lo_s, 1)
            for m in range(KC):
                lora_step(0, m)
            transpose_hg(1)
            pe.wait_ge(hx_out, TILES)
            for k in range(KC):
                l0_step(1, 2, k)
            pe.wait_ge(hgT_lo_s, 2)
            for m in range(KC - 1):
                lora_step(1, m)
            pe.wait_ge(y_lo, 1)
            for k in range(KC):
                l0_step(1, KC - 1, k)
            lora_step(1, KC - 1)
            pe.wait_ge(y_lo, KC)
            for k in range(2):
                pe.wait_ge(w1_lo0_s, k + 1)
                for o in range(KC):
                    l1_step(L1_BANK[0][o], 0, o, k)
            for o in range(KC - 1):
                pe.wait_ge(y_lo, KC + max(o + 1, 2))
                for k in range(2):
                    l1_step(L1_BANK[1][o], 1, o, k)
            for k in range(2, KC):
                pe.wait_ge(w1_lo1_s, k - 1)
                for o in range(KC):
                    last = l1_step(L1_BANK[0][o], 0, o, k)
                    if k == KC - 1:
                        last.then_inc(l1_mm, 1)
            pe.wait_ge(y_lo, 2 * KC)
            for o in range(KC - 1):
                l1_step(L1_BANK[1][o], 1, o, 2)
                l1_step(L1_BANK[1][o], 1, o, 3).then_inc(l1_mm, 1)
            for n in range(2):
                pe.wait_ge(out_s, n + 1)
                for k in range(KC):
                    last = l1_step(LAST_BANK[n], 1, KC - 1, k, OUT_PIECES[LAST_PIECE + n][2])
                last.then_inc(l1_mm, 1)


def kernel(x, itok_B_0_7, condB_scale, itok_Bx4096x4096_0_255, condB_wscale, itok_Bx4096_0_255, condB_bscale,
           _lenS, L0_cond_W, L0_cond_Wr, L0_cond_A, L0_cond_B, L1_cond_weight, L1_cond_bias):
    import numpy as np
    import concourse.bacc as bacc
    from concourse import mybir as mb
    from concourse.bass_utils import run_bass_kernel_spmd

    def rows_on_partitions(m):
        return np.asarray(m).reshape(KC, P, -1).transpose(1, 0, 2)

    def every_partition(v):
        return np.broadcast_to(np.asarray(v), (P, NW))

    x = np.asarray(x)
    ag = np.concatenate([np.asarray(L0_cond_A).reshape(ER, D), np.asarray(L0_cond_Wr)], axis=0)
    wq = np.asarray(itok_Bx4096x4096_0_255)
    arrays = {
        "x_t": x.reshape(HALVES, TH, KC, P).transpose(3, 0, 2, 1),
        "w0_t": rows_on_partitions(np.asarray(L0_cond_W).T),
        "ag_t": rows_on_partitions(ag.T),
        "b_er": np.asarray(L0_cond_B).transpose(0, 2, 1).reshape(ER, D),
        "w1_t": rows_on_partitions(np.asarray(L1_cond_weight).T).reshape(P, PAIRS, PD),
        "wq_t": wq.transpose(2, 0, 1).reshape(PAIRS, 2, P, NW, D).transpose(2, 0, 3, 1, 4).reshape(P, PAIRS, NW, PD),
        "small_f": np.concatenate([every_partition(condB_scale), every_partition(condB_wscale),
                                   every_partition(condB_bscale), np.asarray(L1_cond_bias).reshape(KC, P).T], axis=1),
        "small_i": np.concatenate([every_partition(itok_B_0_7), every_partition(_lenS),
                                   np.asarray(itok_Bx4096_0_255).reshape(NW, KC, P).transpose(2, 1, 0).reshape(P, -1)],
                                  axis=1),
    }
    nc = bacc.Bacc("TRN2", target_bir_lowering=False, num_devices=1)
    args = []
    for name in arrays:
        arrays[name] = np.ascontiguousarray(arrays[name])
        a = arrays[name]
        args.append(nc.dram_tensor(name, a.shape, mb.dt.from_np(a.dtype), kind="ExternalInput").ap())
    out = nc.dram_tensor("out_t", (P, HALVES, KC, TH), mb.dt.float32, kind="ExternalOutput").ap()
    cond_resid_kernel(nc, *args, out)
    r = run_bass_kernel_spmd(nc, [arrays], core_ids=[0])
    out_t = r.results[0]["out_t"]
    return out_t.transpose(1, 3, 2, 0).reshape(BATCH, SEQ, D)
```
